# Optimizing a Trainium2 kernel written in Bass

```python
import numpy as np
import jax
import jax.numpy as jnp

def _softmax(x, axis=-1):
    return jax.nn.softmax(x, axis=axis)

def _gelu(x):
    return jax.nn.gelu(x, approximate=True)

def _silu(x):
    return jax.nn.silu(x)

def _sigmoid(x):
    return jax.nn.sigmoid(x)

def _layernorm(x, axis=-1, eps=1e-05):
    m = jnp.mean(x, axis=axis, keepdims=True)
    v = jnp.var(x, axis=axis, keepdims=True)
    return (x - m) / jnp.sqrt(v + eps)

def _scatter_add(tgt, idx, src, axis=0):
    return tgt.at[idx].add(src)

def _segment_sum(src, seg, n):
    return jax.ops.segment_sum(src, seg, n)
kernel_name = 'mk_adj_preln_d2_adj_r2_f3b90c'

def setup_inputs(seed: int=0):
    np.random.seed(seed)
    _w = jnp.asarray

    def _rec_inputs():
        import jax
        import jax.numpy as jnp
        _gk = jax.random.key(seed)
        x = 0.0002141 + 1 * jax.random.normal(jax.random.fold_in(_gk, 1), (8192, 128), jnp.float32)
        _a = jax.random.bernoulli(jax.random.fold_in(_gk, 2), 0.000244141, (8192, 8192))
        _af = _a.astype(jnp.float32)
        adj = _af
        return (x, adj)
    x, adj = _rec_inputs()

    def _L0_gnn_setup():
        import jax, jax.numpy as jnp
        import numpy as np
        N = 3072
        IN_F = 128
        OUT_F = 128
        H = 4
        OUT_PER_HEAD = OUT_F // H
        ALPHA = 0.2
        NEG_BIG = -9000000000000000.0
        key = jax.random.key(seed)
        k1, k2, k3, k4 = jax.random.split(key, 4)
        h_mat = jax.random.normal(k1, (N, IN_F), dtype=jnp.float32)
        adj = (jax.random.uniform(k2, (N, N)) < 0.05).astype(jnp.float32)
        weight = jax.random.normal(k3, (IN_F, H * OUT_PER_HEAD), dtype=jnp.float32) * (1.0 / np.sqrt(IN_F))
        att_weight = jax.random.normal(k4, (H, 2 * OUT_PER_HEAD), dtype=jnp.float32) * (1.0 / np.sqrt(OUT_PER_HEAD))
        return {'h_mat': h_mat, 'adj': adj, 'weight': weight, 'att_weight': att_weight}
    _L0_gnn_all = _L0_gnn_setup()
    _L0_gnn_in = {k: v for k, v in _L0_gnn_all.items() if k in ('weight', 'att_weight')}
    del _L0_gnn_all

    def _L1_gnn_setup():
        import jax, jax.numpy as jnp
        import numpy as np
        N, DIM = (8192, 128)

        def _gru_cell(x, h, W_ih, W_hh, b_ih, b_hh):
            gi = x @ W_ih.T + b_ih
            gh = h @ W_hh.T + b_hh
            i_r, i_z, i_n = jnp.split(gi, 3, axis=-1)
            h_r, h_z, h_n = jnp.split(gh, 3, axis=-1)
            r = jax.nn.sigmoid(i_r + h_r)
            z = jax.nn.sigmoid(i_z + h_z)
            n = jnp.tanh(i_n + r * h_n)
            return (1.0 - z) * n + z * h
        key = jax.random.key(seed)
        ks = jax.random.split(key, 8)
        states = jax.random.normal(ks[0], (N, DIM), dtype=jnp.float32)
        adj = jax.random.uniform(ks[1], (N, N), dtype=jnp.float32)
        s = 1.0 / np.sqrt(DIM)
        W_msg = jax.random.uniform(ks[2], (DIM, DIM), minval=-s, maxval=s, dtype=jnp.float32)
        b_msg = jax.random.uniform(ks[3], (DIM,), minval=-s, maxval=s, dtype=jnp.float32)
        W_ih = jax.random.uniform(ks[4], (3 * DIM, DIM), minval=-s, maxval=s, dtype=jnp.float32)
        W_hh = jax.random.uniform(ks[5], (3 * DIM, DIM), minval=-s, maxval=s, dtype=jnp.float32)
        b_ih = jax.random.uniform(ks[6], (3 * DIM,), minval=-s, maxval=s, dtype=jnp.float32)
        b_hh = jax.random.uniform(ks[7], (3 * DIM,), minval=-s, maxval=s, dtype=jnp.float32)
        return {'states': states, 'adj': adj, 'W_msg': W_msg, 'b_msg': b_msg, 'W_ih': W_ih, 'W_hh': W_hh, 'b_ih': b_ih, 'b_hh': b_hh}
    _L1_gnn_all = _L1_gnn_setup()
    _L1_gnn_in = {k: v for k, v in _L1_gnn_all.items() if k in ('W_msg', 'b_msg', 'W_ih', 'W_hh', 'b_ih', 'b_hh')}
    del _L1_gnn_all
    return {'x': x, 'adj': adj, 'L0_gnn_weight': _L0_gnn_in['weight'], 'L0_gnn_att_weight': _L0_gnn_in['att_weight'], 'L1_gnn_W_msg': _L1_gnn_in['W_msg'], 'L1_gnn_b_msg': _L1_gnn_in['b_msg'], 'L1_gnn_W_ih': _L1_gnn_in['W_ih'], 'L1_gnn_W_hh': _L1_gnn_in['W_hh'], 'L1_gnn_b_ih': _L1_gnn_in['b_ih'], 'L1_gnn_b_hh': _L1_gnn_in['b_hh']}

def reference(x, adj, L0_gnn_weight, L0_gnn_att_weight, L1_gnn_W_msg, L1_gnn_b_msg, L1_gnn_W_ih, L1_gnn_W_hh, L1_gnn_b_ih, L1_gnn_b_hh):
    import jax
    import jax.numpy as jnp

    def _L0_gnn_ref(h_mat, adj, weight, att_weight):
        import jax, jax.numpy as jnp
        import numpy as np
        N = 3072
        IN_F = 128
        OUT_F = 128
        H = 4
        OUT_PER_HEAD = OUT_F // H
        ALPHA = 0.2
        NEG_BIG = -9000000000000000.0
        n = h_mat.shape[0]
        wh = jnp.matmul(h_mat, weight).reshape(n, H, OUT_PER_HEAD)
        a_src = att_weight[:, :OUT_PER_HEAD]
        a_dst = att_weight[:, OUT_PER_HEAD:]
        logit_parent = jnp.einsum('nhf,hf->nh', wh, a_src)
        logit_child = jnp.einsum('nhf,hf->nh', wh, a_dst)
        e = jax.nn.leaky_relu(logit_parent[:, None, :] + logit_child[None, :, :], ALPHA)
        att = jnp.where(adj[..., None] > 0, e, NEG_BIG)
        att = jax.nn.softmax(att, axis=1)
        h_prime = jnp.einsum('njh,jhf->nhf', att, wh)
        return h_prime.reshape(n, -1)

    def _L1_gnn_ref(states, adj, W_msg, b_msg, W_ih, W_hh, b_ih, b_hh):
        import jax, jax.numpy as jnp
        import numpy as np
        N, DIM = (8192, 128)

        def _gru_cell(x, h, W_ih, W_hh, b_ih, b_hh):
            gi = x @ W_ih.T + b_ih
            gh = h @ W_hh.T + b_hh
            i_r, i_z, i_n = jnp.split(gi, 3, axis=-1)
            h_r, h_z, h_n = jnp.split(gh, 3, axis=-1)
            r = jax.nn.sigmoid(i_r + h_r)
            z = jax.nn.sigmoid(i_z + h_z)
            n = jnp.tanh(i_n + r * h_n)
            return (1.0 - z) * n + z * h
        agg = adj @ states
        msg = jax.nn.relu(agg @ W_msg.T + b_msg)
        return _gru_cell(msg, states, W_ih, W_hh, b_ih, b_hh)
    h = jnp.maximum(_layernorm(x, axis=-1), 0.0)
    x = x + _L0_gnn_ref(h, adj, L0_gnn_weight, L0_gnn_att_weight)
    h = jnp.maximum(_layernorm(x, axis=-1), 0.0)
    x = x + _L1_gnn_ref(h, adj, L1_gnn_W_msg, L1_gnn_b_msg, L1_gnn_W_ih, L1_gnn_W_hh, L1_gnn_b_ih, L1_gnn_b_hh)
    return x

_drawn_inputs = setup_inputs


def setup_inputs(seed=0):
    import zlib

    import numpy as np

    out = dict(_drawn_inputs(seed))
    spreads = {}
    factors = {'L1_gnn_b_msg': 7.783, 'L1_gnn_b_ih': 3.167, 'L1_gnn_b_hh': 5.64}
    for name, (base, spread) in spreads.items():
        noise = np.random.default_rng([zlib.crc32(name.encode()), seed]).standard_normal(out[name].shape)
        drawn = base * np.exp(spread * noise) if base else spread * noise
        out[name] = jnp.asarray(drawn.astype(out[name].dtype))
    for name, factor in factors.items():
        out[name] = (out[name] * factor).astype(out[name].dtype)
    return out
```

```python
from contextlib import ExitStack

import numpy as np

import concourse.bass as bass
from concourse import mybir

F32 = mybir.dt.float32
BF16 = mybir.dt.bfloat16
I32 = mybir.dt.int32
ALU = mybir.AluOpType
ACT = mybir.ActivationFunctionType
AX = mybir.AxisListType

P = 128
N, D = 8192, 128
H = 4
F = D // H
T = N // P
G = 4
NG = T // G
ALPHA = 0.2
BIG = 9.0e15
EPS = 1e-5

PIECE = N // 2
SLOTS = 4

BITS = 14
IBITS = 10
WORDS = -(-N // BITS)
HALF = WORDS // 2
SEG = [(0, HALF // 2), (HALF // 2, HALF)]
CAND = 4 * 8
LEVELS = 3
K = 16
KR = K - 2
NEI0 = (127 + IBITS) * WORDS
W_DMAS = 4 + 2 * H + 9
TW = D + H

assert WORDS <= 1 << IBITS and BITS + IBITS <= 24 and WORDS == 2 * HALF


def gat_gru_kernel(nc, x, adj, weight, att, W_msg, b_msg, W_ih, W_hh, b_ih, b_hh, out):
    ctx = ExitStack()
    with ctx:
        def sb(name, shape, dt=F32):
            return ctx.enter_context(nc.sbuf_tensor(name, shape, dt))

        def sem(name):
            return ctx.enter_context(nc.semaphore(name))

        wh_table = nc.dram_tensor("wh_table", [N, TW], F32, kind="Internal").ap()
        g_table = nc.dram_tensor("g_table", [N, D], F32, kind="Internal").ap()
        adj_values = adj.rearrange("i (j o) -> (i j) o", o=1)
        x_rows = x.rearrange("(t p) d -> p t d", p=P)
        out_rows = out.rearrange("(t p) d -> p t d", p=P)
        wh_rows = wh_table.rearrange("(t p) d -> p t d", p=P)
        g_rows = g_table.rearrange("(t p) d -> p t d", p=P)

        x1 = sb("x1", [P, T, D])
        rs1 = sb("rs1", [P, T])
        nmr1 = sb("nmr1", [P, T])
        nbr_idx = sb("nbr_idx", [P, T, 3], I32)
        nbr_val = sb("nbr_val", [P, T, 3])
        edge_row = sb("edge_row", [P, T])
        parent = sb("parent", [P, T, H])
        child = sb("child", [P, T, H])
        iota = sb("iota", [P, P])
        iota1 = sb("iota1", [P, P])
        ones1 = sb("ones1", [P, 1])
        pid = sb("pid", [P, 1])
        pid_i = sb("pid_i", [P, 1], I32)
        pid1 = sb("pid1", [P, 1])
        ident = sb("ident", [P, P])
        tri = sb("tri", [P, P])
        bit_w = sb("bit_w", [P, BITS, P], BF16)
        idx_w = sb("idx_w", [64, P], BF16)
        idx_r = sb("idx_r", [64, WORDS], BF16)
        ones_b = sb("ones_b", [96, P], BF16)
        a_blk = sb("a_blk", [P, 2 * H])
        wx = sb("wx", [P, D + 2 * H])
        wxT = sb("wxT", [P, D])
        wT = sb("wT", [P, 7, D])
        b_rows = sb("b_rows", [96, 5 * D], BF16)
        whbar = sb("whbar", [P, D])
        adj_in = sb("adj_in", [P, SLOTS, PIECE])
        ind = sb("ind", [P, 2, N], BF16)
        cand = sb("cand", [P, G, CAND])
        cand_i = sb("cand_i", [P, G, CAND], I32)
        word_i = sb("word_i", [P, G, CAND], I32)
        bits_i = sb("bits_i", [P, G, CAND], I32)
        bits = sb("bits", [P, G, CAND])
        top = sb("top", [P, G, CAND])
        expo = sb("expo", [P, G, CAND], I32)
        taken = sb("taken", [P, G, LEVELS * CAND])
        taken2 = sb("taken2", [P, G, LEVELS * CAND])
        nbr = sb("nbr", [P, G, K])
        first2 = sb("first2", [P, G, 2])
        send = sb("send", [P, G, K])
        rest = sb("rest", [P, G])
        list_end = sb("list_end", [P, G])
        below = sb("below", [P, G, P])
        recv = sb("recv", [P, G, K])
        place = sb("place", [P, G])
        picked = sb("picked", [P, G, KR])
        edge_j = sb("edge_j", [P, G])
        idx = sb("idx", [P, G, 3], I32)
        row_f = sb("row_f", [P, G, 3])
        row_i = sb("row_i", [P, G, 3], I32)
        val_idx = sb("val_idx", [P, G, 3], I32)
        tile_row = sb("tile_row", [P, G])
        tile_low = sb("tile_low", [P, G])
        checks = sb("checks", [P, 4, NG])
        over = sb("over", [P, 8])
        over1 = sb("over1", [P, 1])
        over_f = sb("over_f", [1, 1])
        over_i = sb("over_i", [1, 1], I32)
        valid = sb("valid", [P, 2, G, K])
        valid3 = sb("valid3", [P, 2, G, 3])
        sel = sb("sel", [P, 2, G, KR])
        own = sb("own", [P, 2, G, P])
        ownT = sb("ownT", [P, 2, G, P])
        rows_in = sb("rows_in", [P, 2, G, 3, TW])
        vals_in = sb("vals_in", [P, 2, G, 3])
        mask = sb("mask", [P, G, 3])
        cm = sb("cm", [P, G, 3, H + 1])
        cm_rest = sb("cm_rest", [P, G, KR, H + 1])
        pen = sb("pen", [P, G, K])
        logit_c = sb("logit_c", [P, G, K, H])
        cmax = sb("cmax", [P, G, H])
        smax = sb("smax", [P, G, H])
        pm = sb("pm", [P, G, 2 * H])
        pm3 = sb("pm3", [P, G, 3, 2 * H])
        lg = sb("lg", [P, G * 3, H])
        lg2 = sb("lg2", [P, G * 3, H])
        ex = sb("ex", [P, G * 3, H])
        zsafe = sb("zsafe", [P, G, H])
        rz = sb("rz", [P, G, H])
        none = sb("none", [P, G])
        xb = sb("xb", [P, G, D])
        attn = sb("attn", [P, G, D])
        stats = sb("stats", [P, G, 6])
        mv = sb("mv", [P, G, 2])
        sd = sb("sd", [P, G])
        h2 = sb("h2", [P, G, D])
        hT = sb("hT", [P, 2, G, D])
        t_buf = sb("t_buf", [P, 2, G, TW])
        epsc = sb("epsc", [P, 1])
        g_buf = t_buf
        st0 = sb("st0", [P, T, 6])
        mean0 = sb("mean0", [P, T])
        half0 = sb("half0", [P, T])
        var0 = sb("var0", [P, T])
        sd0 = sb("sd0", [P, T])
        rs0 = sb("rs0", [P, T])
        nmr0 = sb("nmr0", [P, T])
        hsum = sb("hsum", [P, NG])
        hbar = sb("hbar", [P, 1])
        hbar_b = sb("hbar_b", [P, P])
        idx2 = sb("idx2", [P, 2, G, 3], I32)
        arena = adj_in[:, 0, :]

        def carve(k, n=1):
            return arena[:, k * G * D:(k + n) * G * D]

        msg = carve(0).rearrange("p (g d) -> p g d", g=G)
        msgT = carve(1).rearrange("p (g d) -> p g d", g=G)
        h2T = carve(2).rearrange("p (g d) -> p g d", g=G)
        rzt = carve(3, 2).rearrange("p (g d) -> p g d", g=G)
        rh = carve(5).rearrange("p (g d) -> p g d", g=G)
        nt = carve(6).rearrange("p (g d) -> p g d", g=G)
        fin = adj_in[:, 1, 0:2 * G * D].rearrange("p (b g d) -> p b g d", b=2, g=G)
        h2r = adj_in[:, 1, 2 * G * D:4 * G * D].rearrange("p (b g d) -> p b g d", b=2, g=G)

        iota_i = own[:].rearrange("p a g e -> p (a g e)").bitcast(I32)[:, 0:WORDS]
        w_raw = ownT[:].rearrange("p a g e -> p (a g e)")[:, 0:7 * D].rearrange("p (c d) -> p c d", c=7)
        start = rows_in[0:96].rearrange("p a g k c -> p (a g k c)")
        b_raw = start[:, 0:6 * D]
        b_all = start[:, 6 * D:11 * D]
        b_part = start[:, 11 * D:16 * D]
        b_hi = start[:, 16 * D:19 * D].bitcast(BF16)[:, 0:5 * D]
        b_lo = start[:, 19 * D:22 * D].bitcast(BF16)[:, 0:5 * D]
        h_buf = rows_in[:, :, :, 0, 0:D]

        gen = adj_in[:, 2, :]
        adj_row = adj_in[:, 0:2, :].rearrange("p s c -> p (s c)")
        all_rows = ind[:].rearrange("p b c -> p (b c)").bitcast(F32).rearrange("p (t d) -> p t d", t=T)
        gen_max = gen[:, 0:4 * P].rearrange("p (h i) -> p h i", h=H)
        gen_lg = gen[:, 4 * P:8 * P].rearrange("p (h i) -> p h i", h=H)
        gen_pm = gen[:, 8 * P:16 * P].rearrange("p (k i) -> p k i", k=2 * H)
        gen_ex = gen[:, 16 * P:20 * P].rearrange("p (h i) -> p h i", h=H)
        gen_at = gen[:, 20 * P:24 * P].rearrange("p (h i) -> p h i", h=H)
        gen_mask = gen[:, 24 * P:25 * P]
        gen_pen = gen[:, 25 * P:26 * P]
        gen_x = gen[:, 26 * P:27 * P]
        gen_block = gen[:, 27 * P:28 * P]
        gen_acc = adj_in[:, 3, 0:TW]
        gen_rows = adj_in[:, 3, 2 * P:4 * P].rearrange("p (k i) -> p k i", k=2)
        gen_h = adj_in[:, 3, 4 * P:5 * P]
        gen_msg = adj_in[:, 3, 5 * P:6 * P]
        gen_rz = adj_in[:, 3, 6 * P:8 * P]
        gen_n = adj_in[:, 3, 8 * P:9 * P]
        gen_u = adj_in[:, 3, 9 * P:10 * P]
        gen_out = adj_in[:, 3, 10 * P:11 * P]
        gen_cols = adj_in[:, 3, 11 * P:19 * P].rearrange("p (k i) -> p k i", k=2 * H)

        ps = ctx.enter_context(nc.psum_tensor("ps", [P, 8, 512], F32))
        ps_small = ps[:, 4, :]
        ps_off = ps_small[:, 0:G]
        ps_recv = ps_small[:, 16:16 + G * K].rearrange("p (g k) -> p g k", g=G)
        ps_pm = ps_small[:, 96:96 + G * 2 * H].rearrange("p (g k) -> p g k", g=G)
        ps_c = ps_small[:, 160:160 + G * KR * (H + 1)].rearrange("p (g k c) -> p g k c", g=G, k=KR)
        ps_tr = ps[:, 7, :].rearrange("p (g d) -> p g d", g=G)

        x_in = sem("x_in")
        w_in = sem("w_in")
        adj_sem = [sem(f"adj_in{i}") for i in range(SLOTS)]
        iota_done = sem("iota_done")
        const_done = sem("const_done")
        var_done = sem("var_done")
        sd_done = sem("sd_done")
        ln0_done = sem("ln0_done")
        wtr_done = sem("wtr_done")
        wtr_out = sem("wtr_out")
        h_done = sem("h_done")
        htr_done = sem("htr_done")
        hT_done = sem("hT_done")
        wh_done = sem("wh_done")
        table_rows = sem("table_rows")
        table_out = [sem(f"table_out{i}") for i in range(2)]
        hbar_done = sem("hbar_done")
        whbar_mm = sem("whbar_mm")
        act_step = sem("act_step")
        dve_step = sem("dve_step")
        ind_done = sem("ind_done")
        pack_done = sem("pack_done")
        seg_done = sem("seg_done")
        rest_done = sem("rest_done")
        off_done = sem("off_done")
        own_done = sem("own_done")
        recv_mm = sem("recv_mm")
        recv_done = sem("recv_done")
        idx_done = sem("idx_done")
        gathered = [sem(f"gathered{i}") for i in range(2)]
        crest_done = sem("crest_done")
        c_mm = sem("c_mm")
        pm_done = sem("pm_done")
        pm_mm = sem("pm_mm")
        pm3_done = sem("pm3_done")
        lg_done = sem("lg_done")
        ex_done = sem("ex_done")
        weighted = sem("weighted")
        agg_mm = sem("agg_mm")
        var2_done = sem("var2_done")
        sd2_done = sem("sd2_done")
        ln2_done = sem("ln2_done")
        h2_done = sem("h2_done")
        h2tr_mm = sem("h2tr_mm")
        h2T_done = sem("h2T_done")
        g_mm = sem("g_mm")
        g_copied = sem("g_copied")
        g_out = [sem(f"g_out{i}") for i in range(2)]
        over_done = sem("over_done")
        over_mm = sem("over_mm")
        passed_pool = sem("passed_pool")
        passed_dve = sem("passed_dve")
        gen_all = sem("gen_all")
        gen_tile = sem("gen_tile")
        gen_in = sem("gen_in")
        turned = sem("turned")
        block_done = sem("block_done")
        values_done = sem("values_done")
        max_step = sem("max_step")
        max_mm = sem("max_mm")
        cols_done = sem("cols_done")
        cols_mm = sem("cols_mm")
        gen_lg_done = sem("gen_lg_done")
        gen_ex_done = sem("gen_ex_done")
        gen_at_done = sem("gen_at_done")
        gen_mm = sem("gen_mm")
        gen_var = sem("gen_var")
        gen_sd = sem("gen_sd")
        gen_ln = sem("gen_ln")
        gen_h_done = sem("gen_h_done")
        gen_tr = sem("gen_tr")
        gen_rows_done = sem("gen_rows_done")
        gen_g_mm = sem("gen_g_mm")
        gen_g_done = sem("gen_g_done")
        gen_g_out = sem("gen_g_out")
        gen_sum = sem("gen_sum")
        gen_gates = sem("gen_gates")
        gen_rz_done = sem("gen_rz_done")
        gen_rh = sem("gen_rh")
        gen_n_done = sem("gen_n_done")
        gen_final = sem("gen_final")
        gen_stored = sem("gen_stored")
        gen_store_free = sem("gen_store_free")
        h2r_done = sem("h2r_done")
        idx2_done = sem("idx2_done")
        gathered2 = [sem(f"gathered2_{i}") for i in range(2)]
        weighted2 = sem("weighted2")
        agg2_mm = sem("agg2_mm")
        msg_done = sem("msg_done")
        tr2_mm = sem("tr2_mm")
        tr2_done = sem("tr2_done")
        gate_mm = sem("gate_mm")
        rz_done = sem("rz_done")
        rh_done = sem("rh_done")
        n_done = sem("n_done")
        fin_done = sem("fin_done")
        out_done = [sem(f"out_done{i}") for i in range(2)]

        def tiles(t0, n=G):
            return bass.ds(t0, n)

        def tile_of(a, t):
            return a[:, bass.ds(t, 1), :].rearrange("p o d -> p (o d)")

        def schedule(eng, body):
            body(0, 0, "c")
            body(1, 1, "ct")
            body(2, 0, "ctb")
            body(3, 1, "ctbg")
            with eng.Fori(2, NG // 2) as i:
                body(i * 2, 0, "ctbg")
                body(i * 2 + 1, 1, "ctbg")
            body(NG, 0, "tbg")
            body(NG + 1, 1, "bg")
            body(NG + 2, 0, "g")

        with nc.Block() as block:

            @block.sync
            def _(sp):
                sp.dma_start(x1[:], x_rows).then_inc(x_in, 16)
                sp.dma_start(wx[:, 0:D], weight).then_inc(w_in, 16)
                sp.dma_start(w_raw[:, 0, :], W_msg).then_inc(w_in, 16)
                sp.dma_start(w_raw[:, 1:4, :], W_ih.rearrange("(c p) d -> p c d", p=P)).then_inc(w_in, 16)
                sp.dma_start(w_raw[:, 4:7, :], W_hh.rearrange("(c p) d -> p c d", p=P)).then_inc(w_in, 16)
                sp.wait_ge(const_done, 1)
                for h in range(H):
                    rows = slice(h * F, (h + 1) * F)
                    sp.dma_start(a_blk[rows, h:h + 1], att[h, F:2 * F].rearrange("(f o) -> f o", o=1)).then_inc(w_in, 16)
                    sp.dma_start(a_blk[rows, H + h:H + h + 1], att[h, 0:F].rearrange("(f o) -> f o", o=1)).then_inc(w_in, 16)
                for r in (0, 32, 64):
                    sp.dma_start(b_raw[r:r + 1, 0:3 * D], b_ih.rearrange("(o d) -> o d", o=1)).then_inc(w_in, 16)
                    sp.dma_start(b_raw[r:r + 1, 3 * D:6 * D], b_hh.rearrange("(o d) -> o d", o=1)).then_inc(w_in, 16)
                    sp.dma_start(b_all[r:r + 1, 4 * D:5 * D], b_msg.rearrange("(o d) -> o d", o=1)).then_inc(w_in, 16)

                def load(tile, half, slot):
                    sp.dma_start(adj_in[:, slot, :], adj[bass.ds(tile * P, P), half * PIECE:(half + 1) * PIECE]) \
                        .then_inc(adj_sem[slot], 16)

                for n in range(SLOTS):
                    load(n // 2, n % 2, n)
                with sp.Fori(0, T // 2 - 1) as i:
                    for n in range(SLOTS):
                        sp.wait_ge(ind_done, i * SLOTS + n + 1)
                        load(i * 2 + 2 + n // 2, n % 2, n)

            @block.gpsimd
            def _(pool):
                nc.gpsimd.iota(iota_i[:], [[1, WORDS]], base=0, channel_multiplier=0)
                nc.gpsimd.iota(pid_i[:], [[0, 1]], base=0, channel_multiplier=1).then_inc(iota_done, 1)

                def gather(par, s):
                    pool.wait_ge(idx_done, s + 1)
                    pool.sem_inc(passed_pool, 1)
                    for t in range(G):
                        for k in range(3):
                            nc.gpsimd.indirect_dma_start(
                                out=rows_in[:, par, t, k, :], out_offset=None, in_=wh_table,
                                in_offset=bass.IndirectOffsetOnAxis(ap=idx[:, t, k:k + 1], axis=0),
                            ).then_inc(gathered[par], 16)
                            nc.gpsimd.indirect_dma_start(
                                out=vals_in[:, par, t, k:k + 1], out_offset=None, in_=adj_values,
                                in_offset=bass.IndirectOffsetOnAxis(ap=val_idx[:, t, k:k + 1], axis=0),
                            ).then_inc(gathered[par], 16)

                def store(q, par):
                    pool.wait_ge(table_rows, q + 1)
                    pool.dma_start(wh_rows[:, tiles(q * G), :], t_buf[:, par]).then_inc(table_out[par], 16)

                with pool.Fori(0, NG // 2) as i:
                    store(i * 2, 0)
                    store(i * 2 + 1, 1)
                for par in range(2):
                    pool.wait_ge(table_out[par], 16 * (NG // 2))
                gather(0, 0)
                gather(1, 1)
                with pool.Fori(1, NG // 2) as i:
                    for par in range(2):
                        pool.wait_ge(agg_mm, i * 2 + par - 1)
                        gather(par, i * 2 + par)

            @block.scalar
            def _(act):
                act.wait_ge(var_done, 1)
                nc.scalar.activation(sd0[:], var0[:], ACT.Sqrt, bias=epsc[:, 0:1]).then_inc(sd_done, 1)

                def relu0(q, par):
                    act.wait_ge(ln0_done, 1)
                    if not isinstance(q, int) or q >= 2:
                        act.wait_ge(htr_done, q - 1)
                    for t in range(G):
                        ins = nc.scalar.activation(h_buf[:, par, t, :], tile_of(x1, q * G + t),
                                                   ACT.Relu, bias=nmr0[:, tiles(q * G + t, 1)], scale=rs0[:, tiles(q * G + t, 1)])
                    ins.then_inc(h_done, 1)

                def turned0(q, par):
                    act.wait_ge(htr_done, q + 1)
                    if not isinstance(q, int) or q >= 2:
                        act.wait_ge(wh_done, q - 1)
                    nc.scalar.activation(hT[:, par].rearrange("p g d -> p (g d)"), ps[:, (7, 4)[par], :], ACT.Identity,
                                         accum_out=hsum[:, bass.ds(q, 1)]).then_inc(hT_done, 1)

                def ahead0(i):
                    relu0(i * 2 + 1, 1)
                    turned0(i * 2, 0)
                    relu0(i * 2 + 2, 0)
                    turned0(i * 2 + 1, 1)

                relu0(0, 0)
                ahead0(0)
                with act.Fori(1, NG // 2 - 1) as i:
                    ahead0(i)
                relu0(NG - 1, 1)
                turned0(NG - 2, 0)
                turned0(NG - 1, 1)

                def h2_rows(s, par):
                    act.wait_ge(ln2_done, s + 1)
                    for t in range(G):
                        ins = nc.scalar.activation(h2[:, t, :],
                                                   tile_of(x1, s * G + t),
                                                   ACT.Relu, bias=nmr1[:, tiles(s * G + t, 1)], scale=rs1[:, tiles(s * G + t, 1)])
                    ins.then_inc(h2_done, 1)
                    act.wait_ge(h2tr_mm, s + 1)
                    nc.scalar.copy(hT[:, 0], ps_tr).then_inc(h2T_done, 1)
                    act.wait_ge(g_mm, s + 1)
                    if not isinstance(s, int) or s >= 2:
                        act.wait_ge(g_out[par], (s - par) * 8)
                    nc.scalar.copy(g_buf[:, par, :, 0:D], ps_tr).then_inc(g_copied, 1)
                    act.wait_ge(g_copied, s + 1)
                    act.dma_start(g_rows[:, tiles(s * G), :], g_buf[:, par, :, 0:D]).then_inc(g_out[par], 16)

                def spread(s):
                    act.wait_ge(pm_done, s + 1)
                    nc.scalar.copy(pm3[:, :, 0, :], pm[:])
                    nc.scalar.copy(pm3[:, :, 1, :], pm[:])
                    act.wait_ge(pm_mm, s + 1)
                    nc.scalar.copy(pm3[:, :, 2, :], ps_pm).then_inc(pm3_done, 1)

                def received(s):
                    act.wait_ge(recv_mm, s + 1)
                    nc.scalar.copy(recv[:], ps_recv).then_inc(recv_done, 1)

                def exps(s):
                    act.wait_ge(lg_done, s + 1)
                    nc.scalar.activation(ex[:], lg[:], ACT.Exp).then_inc(ex_done, 1)

                def deviation(s):
                    act.wait_ge(var2_done, s + 1)
                    nc.scalar.activation(sd[:], mv[:, :, 1], ACT.Sqrt, bias=epsc[:, 0:1]).then_inc(sd2_done, 1)

                def body(s, par, do):
                    if "g" in do:
                        deviation(s - 3)
                        h2_rows(s - 3, 1 - par)
                    if "t" in do:
                        received(s - 1)
                    if "b" in do:
                        spread(s - 2)
                        exps(s - 2)

                schedule(act, body)

            @block.tensor
            def _(pe):
                pe.wait_ge(const_done, 2)
                pe.wait_ge(w_in, W_DMAS * 16)
                nc.tensor.transpose(ps[:, 5, 0:P], wx[:, 0:D], ident[:]).then_inc(wtr_done, 1)
                for c in range(7):
                    ins = nc.tensor.transpose(ps[:, 6 + c // 4, (c % 4) * P:(c % 4 + 1) * P], w_raw[:, c, :], ident[:])
                ins.then_inc(wtr_done, 1)
                pe.wait_ge(wtr_out, 1)
                nc.tensor.matmul(ps[:, 4, 0:2 * H], wxT[:], a_blk[:], start=True, stop=True).then_inc(wtr_done, 1)
                pe.wait_ge(wtr_out, 4)

                def turn0(q, par):
                    pe.wait_ge(h_done, q + 1)
                    if not isinstance(q, int) or q >= 2:
                        pe.wait_ge(hT_done, q - 1)
                    for t in range(G):
                        ins = nc.tensor.transpose(ps[:, (7, 4)[par], t * P:(t + 1) * P], h_buf[:, par, t, :], ident[:])
                    ins.then_inc(htr_done, 1)

                def project(q, par):
                    pe.wait_ge(hT_done, q + 1)
                    if not isinstance(q, int) or q >= 2:
                        pe.wait_ge(table_rows, q - 1)
                    for t in range(G):
                        ins = nc.tensor.matmul(ps[:, (5, 2)[par] + t // 2, (t % 2) * (TW + H):(t % 2 + 1) * (TW + H)], hT[:, par, t, :], wx[:],
                                               start=True, stop=True)
                    ins.then_inc(wh_done, 1)

                def ahead0(i):
                    turn0(i * 2 + 1, 1)
                    project(i * 2, 0)
                    turn0(i * 2 + 2, 0)
                    project(i * 2 + 1, 1)

                turn0(0, 0)
                ahead0(0)
                with pe.Fori(1, NG // 2 - 1) as i:
                    ahead0(i)
                turn0(NG - 1, 1)
                project(NG - 2, 0)
                project(NG - 1, 1)
                pe.wait_ge(hbar_done, 1)
                pe.wait_ge(table_rows, NG)
                nc.tensor.matmul(ps[:, 5, 0:D], hbar_b[:], wx[:, 0:D], start=True, stop=True).then_inc(whbar_mm, 1)

                def pack(s, t):
                    tile = s * G + t
                    pe.wait_ge(ind_done, tile * 2 + 2)
                    if not isinstance(tile, int) or tile >= 2:
                        pe.wait_ge(seg_done, tile - 1)
                    for u in range(2):
                        o = ps[:, (t % 2) * 2 + u, 0:HALF]
                        nc.tensor.matmul(o, idx_w[:], idx_r[:, u * HALF:(u + 1) * HALF], start=True, stop=False)
                        for b in range(BITS):
                            c0 = b * WORDS + u * HALF
                            w = min(HALF, N - c0)
                            ins = nc.tensor.matmul(o[:, 0:w], bit_w[:, b, :], ind[:, t % 2, c0:c0 + w],
                                                   start=False, stop=(b == BITS - 1))
                    ins.then_inc(pack_done, 1)

                def rest_logits(s, par, busy):
                    pe.wait_ge(crest_done, s + 1)
                    if busy:
                        pe.wait_ge(recv_done, s + 2)
                    for t in range(G):
                        ins = nc.tensor.matmul(ps_c[:, t].rearrange("p k c -> p (k c)"), ownT[:, par, t, :],
                                               cm_rest[:, t].rearrange("p k c -> p (k c)"), start=True, stop=True)
                    ins.then_inc(c_mm, 1)

                def list_places(s, busy):
                    pe.wait_ge(rest_done, s + 1)
                    if busy:
                        pe.wait_ge(pm3_done, s - 1)
                    nc.tensor.matmul(ps_off, tri[:], rest[:], start=True, stop=True).then_inc(off_done, 1)

                def maxima(s, par):
                    pe.wait_ge(pm_done, s + 1)
                    for t in range(G):
                        ins = nc.tensor.matmul(ps_pm[:, t, :], own[:, par, t, :], pm[:, t, :], start=True, stop=True)
                    ins.then_inc(pm_mm, 1)

                def send_lists(s, par):
                    pe.wait_ge(own_done, s + 1)
                    for t in range(G):
                        ins = nc.tensor.matmul(ps_recv[:, t, :], own[:, par, t, :], send[:, t, :], start=True, stop=True)
                    ins.then_inc(recv_mm, 1)

                def aggregate(s, par):
                    pe.wait_ge(weighted, s + 1)
                    for t in range(G):
                        o = ps[:, 5 + t // 2, (t % 2) * TW:(t % 2 + 1) * TW]
                        nc.tensor.matmul(o, ident[:], rows_in[:, par, t, 0, :], start=True, stop=False)
                        nc.tensor.matmul(o, ident[:], rows_in[:, par, t, 1, :], start=False, stop=False)
                        ins = nc.tensor.matmul(o, ownT[:, par, t, :], rows_in[:, par, t, 2, :], start=False, stop=True)
                    ins.then_inc(agg_mm, 1)

                def message_rows(s):
                    pe.wait_ge(h2_done, s + 1)
                    if not isinstance(s, int) or s >= 1:
                        pe.wait_ge(g_copied, s)
                    for t in range(G):
                        ins = nc.tensor.transpose(ps_tr[:, t, :], h2[:, t, :], ident[:])
                    ins.then_inc(h2tr_mm, 1)
                    pe.wait_ge(h2T_done, s + 1)
                    for t in range(G):
                        ins = nc.tensor.matmul(ps_tr[:, t, :], hT[:, 0, t, :], wT[:, 0, :], start=True, stop=True)
                    ins.then_inc(g_mm, 1)

                def body(s, par, do):
                    if "c" in do:
                        pack(s, 0)
                    if "g" in do:
                        aggregate(s - 3, 1 - par)
                    if "c" in do:
                        pack(s, 1)
                    if "t" in do:
                        list_places(s - 1, "g" in do)
                    if "g" in do:
                        message_rows(s - 3)
                    if "t" in do:
                        send_lists(s - 1, 1 - par)
                    if "c" in do:
                        pack(s, 2)
                    if "b" in do:
                        rest_logits(s - 2, par, "t" in do)
                        maxima(s - 2, par)
                    if "c" in do:
                        pack(s, 3)

                schedule(pe, body)
                pe.wait_ge(over_done, 1)
                nc.tensor.transpose(ps[0:1, 0, 0:P], over1[:], ident[:]).then_inc(over_mm, 1)

            @block.vector
            def _(dve):
                V = nc.vector
                steps = [0]

                def link(ins):
                    steps[0] += 1
                    ins.then_inc(dve_step, 1)
                    dve.wait_ge(dve_step, steps[0])

                def restart():
                    dve.sem_clear(dve_step)
                    steps[0] = 0

                link(V.memset(a_blk[:], 0.0))
                link(V.memset(b_raw[:], 0.0))
                V.memset(b_all[:], 0.0).then_inc(const_done, 1)
                V.memset(epsc[:], EPS)
                V.memset(ones_b[:], 1.0)
                V.memset(ones1[:], 1.0)
                V.memset(idx_w[:], 0.0)
                link(V.memset(idx_r[:], 0.0))
                V.memset(idx_w[0:1, :], 256.0)
                V.memset(idx_w[32:33, :], 1.0)
                dve.wait_ge(iota_done, 1)
                V.tensor_copy(iota[:], iota_i[:, 0:P])
                V.tensor_copy(pid[:], pid_i[:])
                scratch = ind[:, 0, :].bitcast(I32)[:, 0:WORDS]
                link(V.tensor_scalar(scratch[0:1, :], iota_i[0:1, :], 8, None, ALU.logical_shift_right))
                link(V.tensor_copy(idx_r[0:1, :], scratch[0:1, :]))
                link(V.tensor_scalar(scratch[32:33, :], iota_i[32:33, :], 255, None, ALU.bitwise_and))
                link(V.tensor_copy(idx_r[32:33, :], scratch[32:33, :]))
                V.tensor_scalar(iota1[:], iota[:], 1.0, None, ALU.add)
                V.tensor_scalar(pid1[:], pid[:], 1.0, None, ALU.add)
                V.tensor_scalar(ident[:], iota[:], pid[:, 0:1], None, ALU.is_equal)
                link(V.tensor_scalar(tri[:], iota[:], pid[:, 0:1], None, ALU.is_gt))
                for b in range(BITS):
                    V.tensor_scalar(bit_w[:, b, :], ident[:], float(1 << (b + IBITS)), None, ALU.mult)
                for t in range(G):
                    V.tensor_copy(send[:, t, K - 1:K], pid1[:])
                    V.tensor_scalar(tile_row[:, t:t + 1], pid[:], float(t * P), None, ALU.add)
                    ins = V.memset(tile_low[:, t:t + 1], float(t * P - 1))
                ins.then_inc(const_done, 1)
                dve.wait_ge(w_in, W_DMAS * 16)
                V.tensor_tensor(b_all[:, 0:2 * D], b_raw[:, 0:2 * D], b_raw[:, 3 * D:5 * D], ALU.add)
                V.tensor_copy(b_all[:, 2 * D:3 * D], b_raw[:, 2 * D:3 * D])
                link(V.tensor_copy(b_all[:, 3 * D:4 * D], b_raw[:, 5 * D:6 * D]))
                link(V.tensor_copy(b_hi[:], b_all[:]))
                link(V.tensor_copy(b_rows[:], b_hi[:]))
                link(V.tensor_tensor(b_part[:], b_all[:], b_hi[:], ALU.subtract))
                link(V.tensor_copy(b_lo[:], b_part[:]))
                link(V.tensor_copy(b_rows[32:64, :], b_lo[32:64, :]))
                link(V.tensor_tensor(b_part[:], b_part[:], b_lo[:], ALU.subtract))
                link(V.tensor_copy(b_rows[64:96, :], b_part[64:96, :]))
                dve.wait_ge(x_in, 16)
                with dve.Fori(0, T // 16) as i:
                    for t in range(16):
                        ins = V.bn_stats(st0[:, tiles(i * 16 + t, 1), :].rearrange("p o s -> p (o s)"), tile_of(x1, i * 16 + t))
                link(V.memset(hbar_b[:], 1.0 / N))
                link(V.tensor_tensor(mean0[:], st0[:, :, 1], st0[:, :, 4], ALU.add))
                link(V.tensor_tensor(half0[:], st0[:, :, 1], st0[:, :, 4], ALU.subtract))
                link(V.tensor_tensor(var0[:], st0[:, :, 2], st0[:, :, 5], ALU.add))
                link(V.tensor_tensor(half0[:], half0[:], half0[:], ALU.mult))
                link(V.tensor_scalar(half0[:], half0[:], 0.25, None, ALU.mult))
                V.scalar_tensor_tensor(out=var0[:], in0=var0[:], scalar=1.0 / D, in1=half0[:], op0=ALU.mult, op1=ALU.add) \
                    .then_inc(var_done, 1)
                dve.wait_ge(sd_done, 1)
                link(V.reciprocal(rs0[:], sd0[:]))
                V.scalar_tensor_tensor(out=nmr0[:], in0=mean0[:], scalar=-0.5, in1=rs0[:], op0=ALU.mult, op1=ALU.mult) \
                    .then_inc(ln0_done, 1)
                dve.wait_ge(wtr_done, 1)
                V.tensor_copy(wxT[:], ps[:, 5, 0:P]).then_inc(wtr_out, 1)
                dve.wait_ge(wtr_done, 2)
                V.tensor_copy(wT[:, 0:4, :], ps[:, 6, :].rearrange("p (c d) -> p c d", c=4)).then_inc(wtr_out, 1)
                V.tensor_copy(wT[:, 4:7, :], ps[:, 7, 0:3 * D].rearrange("p (c d) -> p c d", c=3)).then_inc(wtr_out, 1)
                dve.wait_ge(wtr_done, 3)
                V.tensor_copy(wx[:, D:D + 2 * H], ps[:, 4, 0:2 * H]).then_inc(wtr_out, 1)

                def table(q, par):
                    dve.wait_ge(wh_done, q + 1)
                    if not isinstance(q, int):
                        dve.wait_ge(table_out[par], (q - par) * 8)
                    bank = (5, 2)[par]
                    v = ps[:, bank:bank + 2, 0:2 * (TW + H)].rearrange("p b (t c) -> p b t c", t=2)
                    V.tensor_copy(parent[:, tiles(q * G), :].rearrange("p (b t) h -> p b t h", b=2), v[:, :, :, TW:TW + H])
                    V.tensor_copy(child[:, tiles(q * G), :].rearrange("p (b t) h -> p b t h", b=2), v[:, :, :, D:TW])
                    V.tensor_copy(t_buf[:, par].rearrange("p (b t) c -> p b t c", b=2), v[:, :, :, 0:TW]) \
                        .then_inc(table_rows, 1)

                def indicate(s, t):
                    tile = s * G + t
                    if not isinstance(tile, int) or tile >= 2:
                        dve.wait_ge(pack_done, tile - 1)
                    for half in range(2):
                        slot = (2 * t + half) % SLOTS
                        dve.wait_ge(adj_sem[slot], (s * 2 + (2 * t + half) // SLOTS + 1) * 16)
                        V.tensor_scalar(ind[:, t % 2, half * PIECE:(half + 1) * PIECE], adj_in[:, slot, :], 0.0, None,
                                        ALU.not_equal).then_inc(ind_done, 1)

                indicate(0, 0)
                table(0, 0)
                table(1, 1)
                with dve.Fori(1, NG // 2) as i:
                    table(i * 2, 0)
                    table(i * 2 + 1, 1)
                dve.wait_ge(hT_done, NG)
                link(V.tensor_reduce(hbar[:], hsum[:], AX.X, ALU.add))
                V.tensor_scalar(hbar_b[:], hbar_b[:], hbar[:, 0:1], None, ALU.mult).then_inc(hbar_done, 1)
                indicate(0, 1)
                dve.wait_ge(whbar_mm, 1)
                link(V.tensor_copy(whbar[:], ps[:, 5, 0:D]))
                restart()

                def search(s, t):
                    dve.wait_ge(pack_done, s * G + t + 1)
                    dve.sem_inc(passed_dve, 1)
                    for j in range(4):
                        a, b = SEG[j % 2]
                        ins = V.max(cand[:, t, j * 8:(j + 1) * 8], ps[:, (t % 2) * 2 + j // 2, a:b])
                    ins.then_inc(seg_done, 1)

                def decode(s):
                    dve.wait_ge(seg_done, s * G + G)
                    link(V.tensor_copy(cand_i[:], cand[:]))
                    V.tensor_scalar(word_i[:], cand_i[:], (1 << IBITS) - 1, None, ALU.bitwise_and)
                    link(V.tensor_scalar(bits_i[:], cand_i[:], ((1 << BITS) - 1) << IBITS, None, ALU.bitwise_and))
                    link(V.tensor_copy(bits[:], bits_i[:]))
                    for n in range(LEVELS):
                        V.tensor_scalar(top[:].bitcast(I32), bits[:].bitcast(I32), 0x7F800000, None, ALU.bitwise_and)
                        link(V.tensor_scalar(expo[:], bits[:].bitcast(I32), 23, None, ALU.logical_shift_right))
                        V.scalar_tensor_tensor(out=taken[:, :, n * CAND:(n + 1) * CAND], in0=expo[:], scalar=float(WORDS),
                                               in1=word_i[:], op0=ALU.mult, op1=ALU.add)
                        link(V.tensor_tensor(bits[:], bits[:], top[:], ALU.subtract))
                    V.tensor_reduce(checks[:, 0, bass.ds(s, 1)], bits[:].rearrange("p g c -> p (g c)"), AX.X, ALU.max)
                    link(V.tensor_reduce(checks[:, 1, bass.ds(s, 1)], cand[:].rearrange("p g (s e) -> p (g s) e", e=8)[:, :, 7],
                                         AX.X, ALU.max))

                def list_neighbours(s, par):
                    for t in range(G):
                        ins = V.max(nbr[:, t, 0:8], taken[:, t, :])
                    link(ins)
                    for t in range(G):
                        ins = V.match_replace(out=taken2[:, t, :], in_to_replace=nbr[:, t, 0:8], in_values=taken[:, t, :], imm_value=0.0)
                    link(ins)
                    for t in range(G):
                        ins = V.max(nbr[:, t, 8:16], taken2[:, t, :])
                    link(ins)
                    V.tensor_scalar(valid[:, par], nbr[:], float(NEI0), None, ALU.is_ge)
                    V.tensor_scalar(send[:, :, 0:KR], nbr[:, :, 2:K], float(NEI0), 0.0, ALU.subtract, ALU.max)
                    link(V.tensor_scalar(first2[:], nbr[:, :, 0:2], float(NEI0), 0.0, ALU.subtract, ALU.max))
                    V.tensor_reduce(checks[:, 2, bass.ds(s, 1)], nbr[:, :, K - 1], AX.X, ALU.max)
                    V.tensor_reduce(rest[:], valid[:, par, :, 2:K], AX.X, ALU.add).then_inc(rest_done, 1)

                def list_edges(s, par):
                    dve.wait_ge(off_done, s + 1)
                    link(V.tensor_copy(send[:, :, KR], ps_off))
                    link(V.tensor_tensor(list_end[:], rest[:], send[:, :, KR], ALU.add))
                    V.tensor_reduce(checks[:, 3, bass.ds(s, 1)], list_end[:], AX.X, ALU.max)
                    for t in range(G):
                        V.tensor_scalar(below[:, t, :], iota[:], send[:, t, KR:KR + 1], None, ALU.is_lt)
                    link(V.memset(place[:], 0.0))
                    for t in range(G):
                        ins = V.scalar_tensor_tensor(out=own[:, par, t, :], in0=iota[:], scalar=list_end[:, t:t + 1],
                                                     in1=below[:, t, :], op0=ALU.is_lt, op1=ALU.subtract)
                    ins.then_inc(own_done, 1)

                def edge_indices(s, par):
                    dve.wait_ge(recv_done, s + 1)
                    V.tensor_scalar(valid3[:, par, :, 2], recv[:, :, K - 1], 0.0, None, ALU.is_gt)
                    V.tensor_copy(valid3[:, par, :, 0:2], valid[:, par, :, 0:2])
                    link(V.tensor_scalar(place[:], recv[:, :, KR], -1.0, pid[:, 0:1], ALU.mult, ALU.add))
                    link(V.tensor_tensor(sel[:, par], iota[:, 0:KR].unsqueeze(1).to_broadcast([P, G, KR]),
                                         place[:].unsqueeze(2).to_broadcast([P, G, KR]), ALU.is_equal))
                    link(V.tensor_tensor(picked[:], sel[:, par], recv[:, :, 0:KR], ALU.mult))
                    V.tensor_copy(idx[:, :, 0:2], first2[:])
                    V.tensor_copy(row_f[:, :, 0], tile_row[:])
                    V.tensor_copy(row_f[:, :, 1], tile_row[:])
                    link(V.tensor_reduce(edge_j[:], picked[:], AX.X, ALU.add))
                    V.tensor_copy(idx[:, :, 2], edge_j[:])
                    V.tensor_copy(edge_row[:, tiles(s * G)], recv[:, :, K - 1])
                    link(V.tensor_tensor(row_f[:, :, 2], recv[:, :, K - 1], tile_low[:], ALU.add))
                    link(V.tensor_scalar(row_f[:, :, 2], row_f[:, :, 2], 0.0, None, ALU.max))
                    V.tensor_copy(nbr_idx[:, tiles(s * G), :], idx[:])
                    V.tensor_scalar(tile_row[:], tile_row[:], float(G * P), None, ALU.add)
                    V.tensor_scalar(tile_low[:], tile_low[:], float(G * P), None, ALU.add)
                    link(V.tensor_copy(row_i[:], row_f[:]))
                    link(V.tensor_scalar(row_i[:], row_i[:], int(np.log2(N)), None, ALU.logical_shift_left))
                    V.tensor_tensor(val_idx[:], row_i[:], idx[:], ALU.bitwise_or).then_inc(idx_done, 1)
                    for t in range(G):
                        ins = V.tensor_scalar(ownT[:, par, t, :], iota1[:], recv[:, t, K - 1:K], None, ALU.is_equal)
                    link(ins)

                def child_logits(s, par):
                    dve.wait_ge(gathered[par], (s - par) * (3 * G * 2 * 8) + 3 * G * 2 * 16)
                    link(V.tensor_tensor(nbr_val[:, tiles(s * G), :], vals_in[:, par], valid3[:, par], ALU.mult))
                    link(V.tensor_scalar(mask[:], nbr_val[:, tiles(s * G), :], 0.0, None, ALU.is_gt))
                    V.tensor_tensor(cm[:, :, :, 0:H], rows_in[:, par, :, :, D:TW],
                                    mask[:].unsqueeze(3).to_broadcast([P, G, 3, H]), ALU.mult)
                    link(V.tensor_copy(cm[:, :, :, H], mask[:]))
                    V.tensor_tensor(cm_rest[:], sel[:, par].unsqueeze(3).to_broadcast([P, G, KR, H + 1]),
                                    cm[:, :, 2, :].unsqueeze(2).to_broadcast([P, G, KR, H + 1]), ALU.mult) \
                        .then_inc(crest_done, 1)

                def row_maximum(s, par):
                    dve.wait_ge(c_mm, s + 1)
                    V.tensor_scalar(pen[:, :, 0:2], mask[:, :, 0:2], -1.0, BIG, ALU.add, ALU.mult)
                    link(V.tensor_scalar(pen[:, :, 2:K], ps_c[:, :, :, H], -1.0, BIG, ALU.add, ALU.mult))
                    V.tensor_tensor(logit_c[:, :, 0:2, :], cm[:, :, 0:2, 0:H],
                                    pen[:, :, 0:2].unsqueeze(3).to_broadcast([P, G, 2, H]), ALU.add)
                    link(V.tensor_tensor(logit_c[:, :, 2:K, :], ps_c[:, :, :, 0:H],
                                         pen[:, :, 2:K].unsqueeze(3).to_broadcast([P, G, KR, H]), ALU.add))
                    V.tensor_copy(pm[:, :, 0:H], parent[:, tiles(s * G), :])
                    link(V.tensor_reduce(cmax[:], logit_c[:].rearrange("p g k h -> p g h k"), AX.X, ALU.max))
                    link(V.tensor_tensor(smax[:], cmax[:], pm[:, :, 0:H], ALU.add))
                    V.scalar_tensor_tensor(out=pm[:, :, H:2 * H], in0=smax[:], scalar=ALPHA, in1=smax[:],
                                           op0=ALU.mult, op1=ALU.max).then_inc(pm_done, 1)

                def edge_logits(s, par):
                    dve.wait_ge(pm3_done, s + 1)
                    lgv = lg[:].rearrange("p (g k) h -> p g k h", g=G)
                    link(V.tensor_tensor(lgv, rows_in[:, par, :, :, D:TW], pm3[:, :, :, 0:H], ALU.add))
                    link(V.scalar_tensor_tensor(out=lg2[:], in0=lg[:], scalar=ALPHA, in1=lg[:], op0=ALU.mult, op1=ALU.max))
                    link(V.tensor_tensor(lgv, lg2[:].rearrange("p (g k) h -> p g k h", g=G), pm3[:, :, :, H:2 * H], ALU.subtract))
                    V.tensor_scalar(lg[:], lg[:], 0.0, None, ALU.min).then_inc(lg_done, 1)

                def weigh(s, par):
                    dve.wait_ge(ex_done, s + 1)
                    r = rows_in[:, par].rearrange("p g k c -> p (g k) c")
                    link(V.tensor_tensor(r[:, :, D:TW], ex[:],
                                         mask[:].rearrange("p g k -> p (g k)").unsqueeze(2).to_broadcast([P, 3 * G, H]), ALU.mult))
                    rf = r[:, :, 0:D].rearrange("p e (h f) -> p e h f", h=H)
                    V.tensor_tensor(rf, rf, r[:, :, D:TW].unsqueeze(3).to_broadcast([P, 3 * G, H, F]), ALU.mult) \
                        .then_inc(weighted, 1)

                def add_first(s):
                    dve.wait_ge(agg_mm, s + 1)
                    agg = ps[:, 5:7, 0:2 * TW].rearrange("p b (t c) -> p b t c", t=2)
                    link(V.tensor_scalar(zsafe[:].rearrange("p (b t) h -> p b t h", b=2), agg[:, :, :, D:TW], 0.5, None, ALU.max))
                    V.tensor_scalar(none[:].rearrange("p (b t) -> p b t", b=2), agg[:, :, :, D], 0.5, None, ALU.is_lt)
                    link(V.reciprocal(rz[:], zsafe[:]))
                    for b in range(2):
                        V.tensor_tensor(attn[:, 2 * b:2 * b + 2, :].rearrange("p t (h f) -> p t h f", h=H),
                                        agg[:, b, :, 0:D].rearrange("p t (h f) -> p t h f", h=H),
                                        rz[:, 2 * b:2 * b + 2, :].unsqueeze(3).to_broadcast([P, 2, H, F]), ALU.mult)
                    for t in range(G):
                        ins = V.scalar_tensor_tensor(out=xb[:, t, :], in0=whbar[:], scalar=none[:, t:t + 1], in1=tile_of(x1, s * G + t),
                                                     op0=ALU.mult, op1=ALU.add)
                    link(ins)
                    link(V.tensor_tensor(attn[:], attn[:], xb[:], ALU.add))
                    V.tensor_copy(x1[:, tiles(s * G), :], attn[:])
                    for t in range(G):
                        ins = V.bn_stats(stats[:, t, :], attn[:, t, :])
                    link(ins)
                    for t in range(G):
                        ins = V.bn_aggr(mv[:, t, :], stats[:, t, :])
                    ins.then_inc(var2_done, 1)

                def finish_norm(s):
                    dve.wait_ge(sd2_done, s + 1)
                    link(V.reciprocal(rs1[:, tiles(s * G)], sd[:]))
                    V.scalar_tensor_tensor(out=nmr1[:, tiles(s * G)], in0=mv[:, :, 0], scalar=-1.0, in1=rs1[:, tiles(s * G)], op0=ALU.mult, op1=ALU.mult) \
                        .then_inc(ln2_done, 1)

                def body(s, par, do):
                    begun = isinstance(s, int) and s == 0
                    if "c" in do and not begun:
                        indicate(s, 0)
                    if "g" in do:
                        weigh(s - 3, 1 - par)
                    if "t" in do:
                        search(s - 1, 3)
                        decode(s - 1)
                    if "c" in do and not begun:
                        indicate(s, 1)
                    if "g" in do:
                        add_first(s - 3)
                    if "c" in do:
                        search(s, 0)
                    if "t" in do:
                        list_neighbours(s - 1, 1 - par)
                    if "g" in do:
                        finish_norm(s - 3)
                    if "c" in do:
                        indicate(s, 2)
                    if "t" in do:
                        list_edges(s - 1, 1 - par)
                    if "c" in do:
                        search(s, 1)
                    if "b" in do:
                        child_logits(s - 2, par)
                    if "t" in do:
                        edge_indices(s - 1, 1 - par)
                    if "c" in do:
                        indicate(s, 3)
                    if "b" in do:
                        row_maximum(s - 2, par)
                    if "c" in do:
                        search(s, 2)
                    if "b" in do:
                        edge_logits(s - 2, par)
                    if steps[0]:
                        restart()

                schedule(dve, body)
                link(V.tensor_reduce(over[:, 0:4], checks[:], AX.X, ALU.max))
                for n, bound in enumerate((0.5, float(1 << IBITS), float(NEI0), P + 0.5)):
                    ins = V.tensor_scalar(over[:, 4 + n:5 + n], over[:, n:n + 1], bound, None, ALU.is_ge)
                link(ins)
                V.tensor_reduce(over1[:], over[:, 4:8], AX.X, ALU.max).then_inc(over_done, 1)
                dve.wait_ge(over_mm, 1)
                link(V.tensor_reduce(over_f[:], ps[0:1, 0, 0:P], AX.X, ALU.max))
                link(V.tensor_copy(over_i[:], over_f[:]))
                restart()

        with nc.Block() as block:

            @block.sync
            def _(sp):
                general = sp.value_load(over_i[0:1, 0:1], min_val=0, max_val=1)
                with sp.If(general > 0):
                    sp.dma_start(all_rows, wh_rows[:, :, 0:D]).then_inc(gen_all, 16)
                    with sp.Fori(0, T) as i:
                        sp.wait_ge(gen_tile, i + 1)
                        sp.dma_start(adj_row, adj[bass.ds(i * P, P), :]).then_inc(gen_in, 16)
                        sp.dma_start(gen_x, x[bass.ds(i * P, P), :]).then_inc(gen_in, 16)
                    sp.wait_ge(gen_tile, T + 1)
                    sp.dma_start(all_rows, g_rows).then_inc(gen_all, 16)
                    with sp.Fori(0, T) as i:
                        sp.wait_ge(gen_tile, i + (T + 1))
                        sp.dma_start(adj_row, adj[bass.ds(i * P, P), :]).then_inc(gen_in, 16)
                        sp.wait_ge(gen_final, i + 1)
                        sp.dma_start(out[bass.ds(i * P, P), :], gen_out).then_inc(gen_stored, 16)
                    sp.wait_ge(gen_stored, 16 * T)
                with sp.Else():
                    with sp.Fori(0, NG // 2) as i:
                        for par in range(2):
                            sp.wait_ge(fin_done, i * 2 + par + 1)
                            sp.dma_start(out_rows[:, tiles((i * 2 + par) * G), :], fin[:, par]).then_inc(out_done[par], 16)
                    for par in range(2):
                        sp.wait_ge(out_done[par], 16 * (NG // 2))

            @block.gpsimd
            def _(pool):
                general = pool.value_load(over_i[0:1, 0:1], min_val=0, max_val=1)
                with pool.If(general > 0):
                    pool.sem_inc(passed_pool, 1)
                with pool.Else():
                    def gather(q, par):
                        pool.wait_ge(idx2_done, q + 1)
                        pool.sem_inc(passed_pool, 1)
                        for t in range(G):
                            for k in range(3):
                                nc.gpsimd.indirect_dma_start(
                                    out=rows_in[:, par, t, k, 0:D], out_offset=None, in_=g_table,
                                    in_offset=bass.IndirectOffsetOnAxis(ap=idx2[:, par, t, k:k + 1], axis=0),
                                ).then_inc(gathered2[par], 16)

                    for par in range(2):
                        pool.wait_ge(g_out[par], 16 * (NG // 2))
                    gather(0, 0)
                    gather(1, 1)
                    with pool.Fori(1, NG // 2) as i:
                        for par in range(2):
                            pool.wait_ge(agg2_mm, i * 2 + par - 1)
                            gather(i * 2 + par, par)

            @block.vector
            def _(dve):
                V = nc.vector
                steps = [0]

                def link(ins):
                    steps[0] += 1
                    ins.then_inc(dve_step, 1)
                    dve.wait_ge(dve_step, steps[0])

                def restart():
                    dve.sem_clear(dve_step)
                    steps[0] = 0

                def column(a, i):
                    return a[:, bass.ds(i, 1), :].rearrange("p o h -> p (o h)")

                def stage(b):
                    V.tensor_copy(gen_block, adj_row[:, bass.ds(b * P, P)]).then_inc(block_done, 1)

                general = dve.value_load(over_i[0:1, 0:1], min_val=0, max_val=1)
                with dve.If(general > 0):
                    dve.sem_inc(gen_tile, 1)
                    dve.sem_inc(gen_store_free, 1)
                    with dve.Fori(0, T) as i:
                        link(V.memset(gen_max, -BIG))
                        link(V.memset(gen_acc, 0.0))
                        restart()
                        dve.wait_ge(gen_in, i * 32 + 32)
                        dve.sem_inc(passed_dve, 1)
                        with dve.Fori(0, T) as b:
                            stage(b)
                            dve.wait_ge(turned, i * (2 * T) + b + 1)
                            link(V.tensor_scalar(gen_mask, ps[:, 0, 0:P], 0.0, None, ALU.is_gt))
                            link(V.tensor_scalar(gen_pen, gen_mask, -1.0, BIG, ALU.add, ALU.mult))
                            for h in range(H):
                                ins = V.scalar_tensor_tensor(out=gen_max[:, h, :], in0=gen_pen, scalar=child[:, bass.ds(b, 1), h],
                                                             in1=gen_max[:, h, :], op0=ALU.add, op1=ALU.max)
                            link(ins)
                            restart()
                        V.memset(over[:], 0.0).then_inc(max_step, 1)
                        dve.wait_ge(max_mm, i + 1)
                        link(V.tensor_reduce(cmax[:, 0, :], ps[:, 1, :].rearrange("p (h j) -> p h j", h=H), AX.X, ALU.max))
                        V.tensor_copy(pm[:, 0, 0:H], column(parent, i))
                        link(V.tensor_tensor(smax[:, 0, :], cmax[:, 0, :], column(parent, i), ALU.add))
                        link(V.scalar_tensor_tensor(out=pm[:, 0, H:2 * H], in0=smax[:, 0, :], scalar=ALPHA, in1=smax[:, 0, :],
                                                    op0=ALU.mult, op1=ALU.max))
                        link(V.tensor_scalar(gen_cols, pm[:, 0, :].unsqueeze(2).to_broadcast([P, 2 * H, P]), 1.0, None, ALU.mult))
                        V.memset(over[:], 0.0).then_inc(cols_done, 1)
                        dve.wait_ge(cols_mm, i + 1)
                        link(V.tensor_copy(gen_pm[:, 0:H, :], ps[:, 2, :].rearrange("p (k i) -> p k i", k=H)))
                        link(V.tensor_copy(gen_pm[:, H:2 * H, :], ps[:, 3, :].rearrange("p (k i) -> p k i", k=H)))
                        restart()
                        with dve.Fori(0, T) as b:
                            stage(b)
                            dve.wait_ge(turned, i * (2 * T) + b + (T + 1))
                            link(V.tensor_scalar(gen_mask, ps[:, 0, 0:P], 0.0, None, ALU.is_gt))
                            for h in range(H):
                                ins = V.tensor_scalar(gen_lg[:, h, :], gen_pm[:, h, :], child[:, bass.ds(b, 1), h], None, ALU.add)
                            link(ins)
                            link(V.scalar_tensor_tensor(out=gen_lg, in0=gen_lg, scalar=ALPHA, in1=gen_lg, op0=ALU.mult, op1=ALU.max))
                            link(V.tensor_tensor(gen_lg, gen_lg, gen_pm[:, H:2 * H, :], ALU.subtract))
                            V.tensor_scalar(gen_lg, gen_lg, 0.0, None, ALU.min).then_inc(gen_lg_done, 1)
                            dve.wait_ge(gen_ex_done, i * T + b + 1)
                            V.tensor_tensor(gen_at, gen_ex, gen_mask.unsqueeze(1).to_broadcast([P, H, P]), ALU.mult) \
                                .then_inc(gen_at_done, 1)
                            dve.wait_ge(gen_mm, i * T + b + 1)
                            link(V.tensor_tensor(gen_acc, gen_acc, ps[:, 4, 0:TW], ALU.add))
                            restart()
                        link(V.tensor_scalar(zsafe[:, 0, :], gen_acc[:, D:TW], 0.5, None, ALU.max))
                        V.tensor_scalar(none[:, 0:1], gen_acc[:, D:D + 1], 0.5, None, ALU.is_lt)
                        link(V.reciprocal(rz[:, 0, :], zsafe[:, 0, :]))
                        link(V.tensor_tensor(attn[:, 0, :].rearrange("p (h f) -> p h f", h=H), gen_acc[:, 0:D].rearrange("p (h f) -> p h f", h=H),
                                             rz[:, 0, :].unsqueeze(2).to_broadcast([P, H, F]), ALU.mult))
                        link(V.scalar_tensor_tensor(out=xb[:, 0, :], in0=whbar[:], scalar=none[:, 0:1], in1=gen_x, op0=ALU.mult, op1=ALU.add))
                        link(V.tensor_tensor(attn[:, 0, :], attn[:, 0, :], xb[:, 0, :], ALU.add))
                        V.tensor_copy(tile_of(x1, i), attn[:, 0, :])
                        link(V.bn_stats(stats[:, 0, :], attn[:, 0, :]))
                        V.bn_aggr(mv[:, 0, :], stats[:, 0, :]).then_inc(gen_var, 1)
                        dve.wait_ge(gen_sd, i + 1)
                        link(V.reciprocal(rs1[:, tiles(i, 1)], sd[:, 0:1]))
                        V.scalar_tensor_tensor(out=nmr1[:, tiles(i, 1)], in0=mv[:, 0, 0:1], scalar=-1.0, in1=rs1[:, tiles(i, 1)],
                                               op0=ALU.mult, op1=ALU.mult).then_inc(gen_ln, 1)
                        restart()
                    with dve.Fori(0, T) as i:
                        link(V.memset(gen_acc, 0.0))
                        restart()
                        dve.wait_ge(gen_in, i * 16 + (T * 32 + 16))
                        dve.sem_inc(passed_dve, 1)
                        with dve.Fori(0, T) as b:
                            stage(b)
                            dve.wait_ge(turned, i * T + b + (2 * T * T + 1))
                            V.tensor_copy(gen_mask, ps[:, 0, 0:P]).then_inc(values_done, 1)
                            dve.wait_ge(gen_mm, i * T + b + (T * T + 1))
                            link(V.tensor_tensor(gen_acc[:, 0:D], gen_acc[:, 0:D], ps[:, 4, 0:D], ALU.add))
                            restart()
                        link(V.memset(over[:], 0.0))
                        V.memset(over[:], 0.0).then_inc(gen_sum, 1)
                        dve.wait_ge(gen_rz_done, i + 1)
                        link(V.scalar_tensor_tensor(out=gen_u, in0=gen_rz[:, 0:D], scalar=1.0, in1=ps[:, 5, 3 * D:4 * D], op0=ALU.add, op1=ALU.mult))
                        V.scalar_tensor_tensor(out=gen_u, in0=gen_u, scalar=0.5, in1=ps[:, 5, 2 * D:3 * D], op0=ALU.mult, op1=ALU.add) \
                            .then_inc(gen_rh, 1)
                        dve.wait_ge(gen_n_done, i + 1)
                        link(V.tensor_tensor(gen_u, gen_h, gen_n, ALU.subtract))
                        V.tensor_tensor(gen_pen, gen_n, tile_of(x1, i), ALU.add)
                        link(V.scalar_tensor_tensor(out=gen_u, in0=gen_rz[:, D:2 * D], scalar=1.0, in1=gen_u, op0=ALU.add, op1=ALU.mult))
                        dve.wait_ge(gen_store_free, i + 1)
                        V.scalar_tensor_tensor(out=gen_out, in0=gen_u, scalar=0.5, in1=gen_pen, op0=ALU.mult, op1=ALU.add) \
                            .then_inc(gen_final, 1)
                        dve.wait_ge(gen_stored, i * 16 + 16)
                        dve.sem_inc(gen_store_free, 1)
                        dve.sem_inc(gen_tile, 1)
                        restart()
                with dve.Else():
                    def indices(q, par):
                        V.tensor_copy(idx2[:, par], nbr_idx[:, tiles(q * G), :]).then_inc(idx2_done, 1)

                    def prepare(q, par):
                        dve.wait_ge(gathered2[par], (q - par) * (3 * G * 8) + 3 * G * 16)
                        for t in range(G):
                            V.tensor_scalar(ownT[:, par, t, :], iota1[:], edge_row[:, tiles(q * G + t, 1)], None, ALU.is_equal)
                        r = rows_in[:, par].rearrange("p g k c -> p (g k) c")[:, :, 0:D]
                        V.tensor_tensor(r, r, nbr_val[:, tiles(q * G), :].rearrange("p g k -> p (g k)").unsqueeze(2)
                                        .to_broadcast([P, 3 * G, D]), ALU.mult).then_inc(weighted2, 1)

                    def gates(q, par):
                        i_n, h_n = ps[:, 0:G, 2 * D:3 * D], ps[:, 0:G, 3 * D:4 * D]
                        dve.wait_ge(rz_done, q + 1)
                        V.scalar_tensor_tensor(out=rh[:], in0=rzt[:, :, 0:D], scalar=1.0, in1=h_n, op0=ALU.add, op1=ALU.mult) \
                            .then_inc(dve_step, 1)
                        dve.wait_ge(dve_step, q * 4 + 1)
                        V.scalar_tensor_tensor(out=rh[:], in0=rh[:], scalar=0.5, in1=i_n, op0=ALU.mult, op1=ALU.add) \
                            .then_inc(rh_done, 1)

                    def finish(q, par):
                        dve.wait_ge(n_done, q + 1)
                        V.tensor_tensor(rh[:], h2r[:, par], nt[:], ALU.subtract).then_inc(dve_step, 1)
                        V.tensor_tensor(nt[:], nt[:], x1[:, tiles(q * G), :], ALU.add)
                        dve.wait_ge(dve_step, q * 4 + 2)
                        V.scalar_tensor_tensor(out=rh[:], in0=rzt[:, :, D:2 * D], scalar=1.0, in1=rh[:], op0=ALU.add, op1=ALU.mult) \
                            .then_inc(dve_step, 1)
                        if not isinstance(q, int) or q >= 2:
                            dve.wait_ge(out_done[par], (q - par) * 8)
                        dve.wait_ge(dve_step, q * 4 + 3)
                        V.scalar_tensor_tensor(out=fin[:, par], in0=rh[:], scalar=0.5, in1=nt[:], op0=ALU.mult, op1=ALU.add) \
                            .then_inc(fin_done, 1)
                        V.memset(place[:], 0.0).then_inc(dve_step, 1)

                    indices(0, 0)
                    indices(1, 1)
                    prepare(0, 0)

                    def body(q, par, more, idx_more):
                        if idx_more:
                            indices(q + 2, par)
                        if more:
                            prepare(q + 1, 1 - par)
                        gates(q, par)
                        finish(q, par)

                    body(0, 0, True, True)
                    body(1, 1, True, True)
                    with dve.Fori(1, NG // 2 - 1) as i:
                        body(i * 2, 0, True, True)
                        body(i * 2 + 1, 1, True, True)
                    body(NG - 2, 0, True, False)
                    body(NG - 1, 1, False, False)

            @block.scalar
            def _(act):
                general = act.value_load(over_i[0:1, 0:1], min_val=0, max_val=1)
                with act.If(general > 0):
                    with act.Fori(0, T) as i:
                        with act.Fori(0, T) as b:
                            act.wait_ge(gen_lg_done, i * T + b + 1)
                            nc.scalar.activation(gen_ex, gen_lg, ACT.Exp).then_inc(gen_ex_done, 1)
                        act.wait_ge(gen_var, i + 1)
                        nc.scalar.activation(sd[:, 0:1], mv[:, 0, 1:2], ACT.Sqrt, bias=epsc[:, 0:1]).then_inc(gen_sd, 1)
                        act.wait_ge(gen_ln, i + 1)
                        nc.scalar.activation(gen_h, tile_of(x1, i), ACT.Relu, bias=nmr1[:, tiles(i, 1)], scale=rs1[:, tiles(i, 1)]) \
                            .then_inc(gen_h_done, 1)
                        act.wait_ge(gen_tr, i + 1)
                        nc.scalar.copy(gen_rows[:, 0, :], ps[:, 6, 0:P]).then_inc(gen_rows_done, 1)
                        act.wait_ge(gen_g_mm, i + 1)
                        nc.scalar.copy(gen_msg, ps[:, 6, 0:P]).then_inc(gen_g_done, 1)
                        act.wait_ge(gen_g_done, i + 1)
                        act.dma_start(g_table[bass.ds(i * P, P), :], gen_msg).then_inc(gen_g_out, 16)
                        act.wait_ge(gen_g_out, i * 16 + 16)
                        act.sem_inc(gen_tile, 1)
                    with act.Fori(0, T) as i:
                        act.wait_ge(gen_tile, i + (T + 1))
                        nc.scalar.activation(gen_h, tile_of(x1, i), ACT.Relu, bias=nmr1[:, tiles(i, 1)], scale=rs1[:, tiles(i, 1)]) \
                            .then_inc(gen_h_done, 1)
                        act.wait_ge(gen_tr, i * 2 + (T + 1))
                        nc.scalar.activation(gen_msg, ps[:, 7, 0:P], ACT.Relu)
                        nc.scalar.copy(gen_rows[:, 0, :], ps[:, 6, 0:P]).then_inc(gen_rows_done, 1)
                        act.wait_ge(gen_tr, i * 2 + (T + 2))
                        nc.scalar.copy(gen_rows[:, 1, :], ps[:, 6, 0:P]).then_inc(gen_rows_done, 1)
                        act.wait_ge(gen_gates, i + 1)
                        nc.scalar.activation(gen_rz, ps[:, 5, 0:2 * D], ACT.Tanh, scale=0.5).then_inc(gen_rz_done, 1)
                        act.wait_ge(gen_rh, i + 1)
                        nc.scalar.activation(gen_n, gen_u, ACT.Tanh).then_inc(gen_n_done, 1)
                with act.Else():
                    def normed(q, par):
                        if not isinstance(q, int) or q >= 2:
                            act.wait_ge(fin_done, q - 1)
                        for t in range(G):
                            ins = nc.scalar.activation(h2r[:, par, t, :], tile_of(x1, q * G + t), ACT.Relu,
                                                       bias=nmr1[:, tiles(q * G + t, 1)], scale=rs1[:, tiles(q * G + t, 1)])
                        ins.then_inc(h2r_done, 1)

                    def body(q, par, more=True):
                        act.wait_ge(agg2_mm, q + 1)
                        nc.scalar.activation(msg[:], ps[:, 6 + par, :].rearrange("p (g d) -> p g d", g=G), ACT.Relu).then_inc(msg_done, 1)
                        act.wait_ge(tr2_mm, q * 2 + 1)
                        nc.scalar.copy(h2T[:], ps[:, 5, :].rearrange("p (g d) -> p g d", g=G)).then_inc(tr2_done, 1)
                        act.wait_ge(tr2_mm, q * 2 + 2)
                        nc.scalar.copy(msgT[:], ps[:, 4, :].rearrange("p (g d) -> p g d", g=G)).then_inc(tr2_done, 1)
                        if more:
                            normed(q + 1, 1 - par)
                        act.wait_ge(gate_mm, q + 1)
                        nc.scalar.activation(rzt[:], ps[:, 0:G, 0:2 * D], ACT.Tanh, scale=0.5).then_inc(rz_done, 1)
                        act.wait_ge(rh_done, q + 1)
                        nc.scalar.activation(nt[:], rh[:], ACT.Tanh).then_inc(n_done, 1)

                    normed(0, 0)
                    body(0, 0)
                    body(1, 1)
                    with act.Fori(1, NG // 2 - 1) as i:
                        body(i * 2, 0)
                        body(i * 2 + 1, 1)
                    body(NG - 2, 0)
                    body(NG - 1, 1, False)

            @block.tensor
            def _(pe):
                general = pe.value_load(over_i[0:1, 0:1], min_val=0, max_val=1)

                def turn(n):
                    pe.wait_ge(block_done, n + 1)
                    nc.tensor.transpose(ps[:, 0, 0:P], gen_block, ident[:]).then_inc(turned, 1)

                with pe.If(general > 0):
                    pe.wait_ge(gen_all, 16)
                    with pe.Fori(0, T) as i:
                        with pe.Fori(0, T) as b:
                            turn(i * (2 * T) + b)
                        pe.wait_ge(max_step, i + 1)
                        for h in range(H):
                            ins = nc.tensor.transpose(ps[:, 1, h * P:(h + 1) * P], gen_max[:, h, :], ident[:])
                        ins.then_inc(max_mm, 1)
                        pe.wait_ge(cols_done, i + 1)
                        for k in range(2 * H):
                            ins = nc.tensor.matmul(ps[:, 2 + k // H, (k % H) * P:(k % H + 1) * P], gen_cols[:, k, :], ident[:],
                                                   start=True, stop=True)
                        ins.then_inc(cols_mm, 1)
                        with pe.Fori(0, T) as b:
                            turn(i * (2 * T) + b + T)
                            pe.wait_ge(gen_at_done, i * T + b + 1)
                            for h in range(H):
                                nc.tensor.matmul(ps[:, 4, h * F:(h + 1) * F], gen_at[:, h, :],
                                                 all_rows[:, bass.ds(b, 1), h * F:(h + 1) * F].rearrange("p o f -> p (o f)"),
                                                 start=True, stop=True)
                                ins = nc.tensor.matmul(ps[:, 4, D + h:D + h + 1], gen_at[:, h, :], ones1[:], start=True, stop=True)
                            ins.then_inc(gen_mm, 1)
                        pe.wait_ge(gen_h_done, i + 1)
                        nc.tensor.transpose(ps[:, 6, 0:P], gen_h, ident[:]).then_inc(gen_tr, 1)
                        pe.wait_ge(gen_rows_done, i + 1)
                        nc.tensor.matmul(ps[:, 6, 0:P], gen_rows[:, 0, :], wT[:, 0, :], start=True, stop=True).then_inc(gen_g_mm, 1)
                    pe.wait_ge(gen_all, 32)
                    with pe.Fori(0, T) as i:
                        with pe.Fori(0, T) as b:
                            turn(i * T + b + 2 * T * T)
                            pe.wait_ge(values_done, i * T + b + 1)
                            nc.tensor.matmul(ps[:, 4, 0:D], gen_mask, tile_of(all_rows, b), start=True, stop=True).then_inc(gen_mm, 1)
                        pe.wait_ge(gen_sum, i + 1)
                        pe.wait_ge(gen_h_done, i + (T + 1))
                        nc.tensor.matmul(ps[:, 7, 0:D], ones_b[:], b_rows[:, 4 * D:5 * D], start=True, stop=False)
                        nc.tensor.matmul(ps[:, 7, 0:D], ident[:], gen_acc[:, 0:D], start=False, stop=True)
                        nc.tensor.transpose(ps[:, 6, 0:P], gen_h, ident[:]).then_inc(gen_tr, 1)
                        pe.wait_ge(gen_rows_done, i * 2 + (T + 1))
                        nc.tensor.transpose(ps[:, 6, 0:P], gen_msg, ident[:]).then_inc(gen_tr, 1)
                        pe.wait_ge(gen_rows_done, i * 2 + (T + 2))
                        o = ps[:, 5, :]
                        nc.tensor.matmul(o, ones_b[:], b_rows[:, 0:4 * D], start=True, stop=False)
                        nc.tensor.matmul(o[:, 0:2 * D], gen_rows[:, 0, :], wT[:, 4:6, :].rearrange("p c d -> p (c d)"), start=False, stop=False)
                        nc.tensor.matmul(o[:, 3 * D:4 * D], gen_rows[:, 0, :], wT[:, 6, :], start=False, stop=False)
                        nc.tensor.matmul(o[:, 0:3 * D], gen_rows[:, 1, :], wT[:, 1:4, :].rearrange("p c d -> p (c d)"),
                                         start=False, stop=True).then_inc(gen_gates, 1)
                with pe.Else():
                    def body(q, par):
                        pe.wait_ge(h2r_done, q + 1)
                        for t in range(G):
                            ins = nc.tensor.transpose(ps[:, 5, t * D:(t + 1) * D], h2r[:, par, t, :], ident[:])
                        ins.then_inc(tr2_mm, 1)
                        pe.wait_ge(weighted2, q + 1)
                        for t in range(G):
                            o = ps[:, 6 + par, t * D:(t + 1) * D]
                            nc.tensor.matmul(o, ones_b[:], b_rows[:, 4 * D:5 * D], start=True, stop=False)
                            nc.tensor.matmul(o, ident[:], rows_in[:, par, t, 0, 0:D], start=False, stop=False)
                            nc.tensor.matmul(o, ident[:], rows_in[:, par, t, 1, 0:D], start=False, stop=False)
                            ins = nc.tensor.matmul(o, ownT[:, par, t, :], rows_in[:, par, t, 2, 0:D], start=False, stop=True)
                        ins.then_inc(agg2_mm, 1)
                        pe.wait_ge(msg_done, q + 1)
                        for t in range(G):
                            ins = nc.tensor.transpose(ps[:, 4, t * D:(t + 1) * D], msg[:, t, :], ident[:])
                        ins.then_inc(tr2_mm, 1)
                        if not isinstance(q, int) or q >= 1:
                            pe.wait_ge(fin_done, q)
                        pe.wait_ge(tr2_done, q * 2 + 2)
                        for t in range(G):
                            o = ps[:, t, :]
                            nc.tensor.matmul(o, ones_b[:], b_rows[:, 0:4 * D], start=True, stop=False)
                            nc.tensor.matmul(o[:, 0:2 * D], h2T[:, t, :], wT[:, 4:6, :].rearrange("p c d -> p (c d)"), start=False, stop=False)
                            nc.tensor.matmul(o[:, 3 * D:4 * D], h2T[:, t, :], wT[:, 6, :], start=False, stop=False)
                            ins = nc.tensor.matmul(o[:, 0:3 * D], msgT[:, t, :], wT[:, 1:4, :].rearrange("p c d -> p (c d)"), start=False, stop=True)
                        ins.then_inc(gate_mm, 1)

                    body(0, 0)
                    body(1, 1)
                    with pe.Fori(1, NG // 2) as i:
                        body(i * 2, 0)
                        body(i * 2 + 1, 1)


_INS = ['x', 'adj', 'L0_gnn_weight', 'L0_gnn_att_weight', 'L1_gnn_W_msg', 'L1_gnn_b_msg', 'L1_gnn_W_ih', 'L1_gnn_W_hh',
        'L1_gnn_b_ih', 'L1_gnn_b_hh']


def kernel(**inputs):
    import numpy as _np
    import concourse.bacc as _bacc
    from concourse import mybir as _mybir
    from concourse.bass_utils import run_bass_kernel_spmd as _run

    nc = _bacc.Bacc("TRN2", target_bir_lowering=False, num_devices=1)
    arrays, args = {}, {}
    for name in _INS:
        a = _np.ascontiguousarray(inputs[name])
        arrays[f"in_{name}"] = a
        args[name] = nc.dram_tensor(f"in_{name}", a.shape, _mybir.dt.from_np(a.dtype), kind="ExternalInput").ap()
    out = nc.dram_tensor("out_0", (N, D), F32, kind="ExternalOutput").ap()
    gat_gru_kernel(nc, args['x'], args['adj'], args['L0_gnn_weight'], args['L0_gnn_att_weight'], args['L1_gnn_W_msg'],
                   args['L1_gnn_b_msg'], args['L1_gnn_W_ih'], args['L1_gnn_W_hh'], args['L1_gnn_b_ih'],
                   args['L1_gnn_b_hh'], out)
    r = _run(nc, [arrays], core_ids=[0])
    return r.results[0]["out_0"]
```
